# Optimizing a Trainium2 kernel written in Bass

```python
import numpy as np
import jax
import jax.numpy as jnp

def _softmax(x, axis=-1):
    return jax.nn.softmax(x, axis=axis)

def _gelu(x):
    return jax.nn.gelu(x, approximate=True)

def _silu(x):
    return jax.nn.silu(x)

def _sigmoid(x):
    return jax.nn.sigmoid(x)

def _layernorm(x, axis=-1, eps=1e-05):
    m = jnp.mean(x, axis=axis, keepdims=True)
    v = jnp.var(x, axis=axis, keepdims=True)
    return (x - m) / jnp.sqrt(v + eps)

def _scatter_add(tgt, idx, src, axis=0):
    return tgt.at[idx].add(src)

def _segment_sum(src, seg, n):
    return jax.ops.segment_sum(src, seg, n)
kernel_name = 'mk_seq_postln_d1_jaxref_r4_78abd4'

def setup_inputs(seed: int=0):
    np.random.seed(seed)
    _w = jnp.asarray

    def _L0_attn_setup():
        import jax, jax.numpy as jnp
        import numpy as np
        N_HEAD = 16
        LATENT = 32

        def _rotate_half(x):
            xe = x[..., ::2]
            xo = x[..., 1::2]
            return jnp.stack((-xo, xe), axis=-1).reshape(x.shape)

        def _rope_tables(T, latent_dim, dtype):
            inv_freq = 1.0 / 10000.0 ** (jnp.arange(0, latent_dim, 2, dtype=jnp.float32) / latent_dim)
            t = jnp.arange(T, dtype=jnp.float32)
            freqs = jnp.outer(t, inv_freq)
            cos = jnp.repeat(jnp.cos(freqs), 2, axis=-1)[:, :latent_dim]
            sin = jnp.repeat(jnp.sin(freqs), 2, axis=-1)[:, :latent_dim]
            return (cos.astype(dtype), sin.astype(dtype))
        key = jax.random.key(seed)
        ks = jax.random.split(key, 14)
        C = 256
        hd = C // N_HEAD
        L = LATENT
        s = 0.02
        return {'x': jax.random.normal(ks[0], (4, 512, C), jnp.float32), 'c_attn_w': jax.random.normal(ks[1], (3 * C, C), jnp.float32) * s, 'c_attn_b': jnp.zeros((3 * C,), jnp.float32), 'q2l_w': jax.random.normal(ks[2], (L, hd), jnp.float32) * s, 'q2l_b': jnp.zeros((L,), jnp.float32), 'kv2l_w': jax.random.normal(ks[3], (L, hd), jnp.float32) * s, 'kv2l_b': jnp.zeros((L,), jnp.float32), 'l2o_w': jax.random.normal(ks[4], (hd, L), jnp.float32) * s, 'l2o_b': jnp.zeros((hd,), jnp.float32), 'wqk_w': jax.random.normal(ks[5], (L, L), jnp.float32) * s, 'wqk_b': jnp.zeros((L,), jnp.float32), 'cproj_w': jax.random.normal(ks[6], (C, C), jnp.float32) * s, 'cproj_b': jnp.zeros((C,), jnp.float32)}
    _L0_attn_in = _L0_attn_setup()

    def _L0_ffn_setup():
        import jax, jax.numpy as jnp
        import numpy as np
        DIM = 256
        E = 8
        K = 2
        EPS = 1e-05

        def _ln(x, g, b):
            mu = jnp.mean(x, axis=-1, keepdims=True)
            var = jnp.mean(jnp.square(x - mu), axis=-1, keepdims=True)
            return (x - mu) * jax.lax.rsqrt(var + EPS) * g + b
        key = jax.random.key(seed)
        ks = jax.random.split(key, 8)
        H = 2 * DIM
        s_in = 1.0 / np.sqrt(DIM)
        s_h = 1.0 / np.sqrt(H)
        return {'x': jax.random.normal(ks[0], (2, 512, DIM), dtype=jnp.float32), 'gate_w': jax.random.uniform(ks[1], (DIM, E), minval=-s_in, maxval=s_in, dtype=jnp.float32), 'w1': jax.random.uniform(ks[2], (E, DIM, H), minval=-s_in, maxval=s_in, dtype=jnp.float32), 'b1': jax.random.uniform(ks[3], (E, H), minval=-s_in, maxval=s_in, dtype=jnp.float32), 'ln1_g': jnp.ones((E, H), dtype=jnp.float32), 'ln1_b': jnp.zeros((E, H), dtype=jnp.float32), 'w2': jax.random.uniform(ks[4], (E, H, DIM), minval=-s_h, maxval=s_h, dtype=jnp.float32), 'b2': jax.random.uniform(ks[5], (E, DIM), minval=-s_h, maxval=s_h, dtype=jnp.float32), 'ln_g': jnp.ones((DIM,), dtype=jnp.float32), 'ln_b': jnp.zeros((DIM,), dtype=jnp.float32)}
    _L0_ffn_in = _L0_ffn_setup()
    _d = {'L0_attn_x': _L0_attn_in['x'], 'L0_attn_c_attn_w': _L0_attn_in['c_attn_w'], 'L0_attn_c_attn_b': _L0_attn_in['c_attn_b'], 'L0_attn_q2l_w': _L0_attn_in['q2l_w'], 'L0_attn_q2l_b': _L0_attn_in['q2l_b'], 'L0_attn_kv2l_w': _L0_attn_in['kv2l_w'], 'L0_attn_kv2l_b': _L0_attn_in['kv2l_b'], 'L0_attn_l2o_w': _L0_attn_in['l2o_w'], 'L0_attn_l2o_b': _L0_attn_in['l2o_b'], 'L0_attn_wqk_w': _L0_attn_in['wqk_w'], 'L0_attn_wqk_b': _L0_attn_in['wqk_b'], 'L0_attn_cproj_w': _L0_attn_in['cproj_w'], 'L0_attn_cproj_b': _L0_attn_in['cproj_b'], 'L0_ffn_gate_w': _L0_ffn_in['gate_w'], 'L0_ffn_w1': _L0_ffn_in['w1'], 'L0_ffn_b1': _L0_ffn_in['b1'], 'L0_ffn_ln1_g': _L0_ffn_in['ln1_g'], 'L0_ffn_ln1_b': _L0_ffn_in['ln1_b'], 'L0_ffn_w2': _L0_ffn_in['w2'], 'L0_ffn_b2': _L0_ffn_in['b2'], 'L0_ffn_ln_g': _L0_ffn_in['ln_g'], 'L0_ffn_ln_b': _L0_ffn_in['ln_b']}
    _x0 = _d['L0_attn_x']
    _d['L0_attn_x'] = jax.random.normal(jax.random.fold_in(jax.random.key(seed), 1), (8, 1024, 256), dtype=_x0.dtype)
    del _x0
    return _d

def reference(L0_attn_x, L0_attn_c_attn_w, L0_attn_c_attn_b, L0_attn_q2l_w, L0_attn_q2l_b, L0_attn_kv2l_w, L0_attn_kv2l_b, L0_attn_l2o_w, L0_attn_l2o_b, L0_attn_wqk_w, L0_attn_wqk_b, L0_attn_cproj_w, L0_attn_cproj_b, L0_ffn_gate_w, L0_ffn_w1, L0_ffn_b1, L0_ffn_ln1_g, L0_ffn_ln1_b, L0_ffn_w2, L0_ffn_b2, L0_ffn_ln_g, L0_ffn_ln_b):

    def _L0_attn_ref(x, c_attn_w, c_attn_b, q2l_w, q2l_b, kv2l_w, kv2l_b, l2o_w, l2o_b, wqk_w, wqk_b, cproj_w, cproj_b):
        import jax, jax.numpy as jnp
        import numpy as np
        N_HEAD = 16
        LATENT = 32

        def _rotate_half(x):
            xe = x[..., ::2]
            xo = x[..., 1::2]
            return jnp.stack((-xo, xe), axis=-1).reshape(x.shape)

        def _rope_tables(T, latent_dim, dtype):
            inv_freq = 1.0 / 10000.0 ** (jnp.arange(0, latent_dim, 2, dtype=jnp.float32) / latent_dim)
            t = jnp.arange(T, dtype=jnp.float32)
            freqs = jnp.outer(t, inv_freq)
            cos = jnp.repeat(jnp.cos(freqs), 2, axis=-1)[:, :latent_dim]
            sin = jnp.repeat(jnp.sin(freqs), 2, axis=-1)[:, :latent_dim]
            return (cos.astype(dtype), sin.astype(dtype))
        B, T, C = x.shape
        H = N_HEAD
        hd = C // H
        L = q2l_w.shape[0]
        qkv = x @ c_attn_w.T + c_attn_b
        q, k, v = jnp.split(qkv, 3, axis=2)

        def heads(t):
            return t.reshape(B, T, H, hd).transpose(0, 2, 1, 3)
        q, k, v = (heads(q), heads(k), heads(v))
        q_lat = q @ q2l_w.T + q2l_b
        k_lat = k @ kv2l_w.T + kv2l_b
        v_lat = v @ kv2l_w.T + kv2l_b
        cos, sin = _rope_tables(T, L, x.dtype)
        cos = cos[None, None]
        sin = sin[None, None]
        q_lat = q_lat * cos + _rotate_half(q_lat) * sin
        k_lat = k_lat * cos + _rotate_half(k_lat) * sin
        q_for_k = q_lat @ wqk_w.T + wqk_b
        att = jnp.einsum('bhql,bhkl->bhqk', q_for_k, k_lat) * L ** (-0.5)
        causal = jnp.tril(jnp.ones((T, T), dtype=bool))
        att = jnp.where(causal[None, None], att, -jnp.inf)
        att = jax.nn.softmax(att, axis=-1)
        y_lat = jnp.einsum('bhqk,bhkl->bhql', att, v_lat)
        y = y_lat @ l2o_w.T + l2o_b
        y = y.transpose(0, 2, 1, 3).reshape(B, T, C)
        return y @ cproj_w.T + cproj_b

    def _L0_ffn_ref(x, gate_w, w1, b1, ln1_g, ln1_b, w2, b2, ln_g, ln_b):
        import jax, jax.numpy as jnp
        import numpy as np
        DIM = 256
        E = 8
        K = 2
        EPS = 1e-05

        def _ln(x, g, b):
            mu = jnp.mean(x, axis=-1, keepdims=True)
            var = jnp.mean(jnp.square(x - mu), axis=-1, keepdims=True)
            return (x - mu) * jax.lax.rsqrt(var + EPS) * g + b
        shape = x.shape
        xf = x.reshape(-1, shape[-1])
        gates = jax.nn.softmax(xf @ gate_w, axis=-1)
        topw, topi = jax.lax.top_k(gates, K)
        topw = topw / jnp.sum(topw, axis=-1, keepdims=True)
        combine = jnp.sum(topw[:, :, None] * jax.nn.one_hot(topi, E, dtype=xf.dtype), axis=1)
        h = jnp.einsum('td,edh->teh', xf, w1) + b1
        h = _ln(h, ln1_g, ln1_b)
        h = jax.nn.gelu(h, approximate=False)
        y = jnp.einsum('teh,ehd->ted', h, w2) + b2
        out = jnp.einsum('ted,te->td', y, combine)
        out = _ln(out + xf, ln_g, ln_b)
        return out.reshape(shape)
    x = L0_attn_x
    x = _layernorm(x + _L0_attn_ref(x, L0_attn_c_attn_w, L0_attn_c_attn_b, L0_attn_q2l_w, L0_attn_q2l_b, L0_attn_kv2l_w, L0_attn_kv2l_b, L0_attn_l2o_w, L0_attn_l2o_b, L0_attn_wqk_w, L0_attn_wqk_b, L0_attn_cproj_w, L0_attn_cproj_b), axis=-1)
    x = _layernorm(x + _L0_ffn_ref(x, L0_ffn_gate_w, L0_ffn_w1, L0_ffn_b1, L0_ffn_ln1_g, L0_ffn_ln1_b, L0_ffn_w2, L0_ffn_b2, L0_ffn_ln_g, L0_ffn_ln_b), axis=-1)
    return x

_drawn_inputs = setup_inputs


def setup_inputs(seed=0):
    import zlib

    import numpy as np

    out = dict(_drawn_inputs(seed))
    spreads = {'L0_attn_c_attn_b': (0.0, 0.8),
     'L0_attn_q2l_b': (0.0, 0.8),
     'L0_attn_kv2l_b': (0.0, 0.8),
     'L0_attn_l2o_b': (0.0, 0.1),
     'L0_attn_wqk_b': (0.0, 0.8),
     'L0_attn_cproj_b': (0.0, 0.1),
     'L0_ffn_ln1_g': (1.0, 0.2),
     'L0_ffn_ln1_b': (0.0, 0.569),
     'L0_ffn_ln_g': (1.0, 0.2),
     'L0_ffn_ln_b': (0.0, 0.1)}
    factors = {'L0_attn_c_attn_w': 8.0,
     'L0_attn_q2l_w': 8.0,
     'L0_attn_kv2l_w': 8.0,
     'L0_attn_l2o_w': 7.786,
     'L0_attn_wqk_w': 8.0,
     'L0_ffn_b1': 6.037,
     'L0_ffn_b2': 5.949}
    for name, (base, spread) in spreads.items():
        noise = np.random.default_rng([zlib.crc32(name.encode()), seed]).standard_normal(out[name].shape)
        drawn = base * np.exp(spread * noise) if base else spread * noise
        out[name] = jnp.asarray(drawn.astype(out[name].dtype))
    for name, factor in factors.items():
        out[name] = (out[name] * factor).astype(out[name].dtype)
    return out
```

```python
from contextlib import ExitStack

import numpy as np
import concourse.bass as bass
from concourse import mybir

F32, F32R, BF16 = mybir.dt.float32, mybir.dt.float32r, mybir.dt.bfloat16
I32, U32 = mybir.dt.int32, mybir.dt.uint32
ACT = mybir.ActivationFunctionType
ALU = mybir.AluOpType
AX_X = mybir.AxisListType.X

P = 128
B, T, C = 8, 1024, 256
NH, HD, L = 16, 16, 32
HG = P // L
GROUPS = NH // HG
KC = C // P
TB = T // P
HALF = 512
E, H = 8, 512
FC = H // P
TILES = B * TB
MAX_TILES = 2 * TILES + E
HALF_TILES = MAX_TILES // 2
CG = 4
EXPERT_LOADS = ("w1", "w2", "ln1_g", "ln1_b")
BF16_BITS = ("ident_bf", "mask", "mask_T", "before", "ones")
EPS = 1e-5
NEG = -1e30
STEPS = [(0, (0, 1)), (0, (2, 3)), (1, (0, 1)), (1, (2, 3)), (1, (4, 5)), (1, (6, 7))]
S_FIRST, S_LAST = 8, 22
A_FIRST = 4
SUM_ROWS = [HD + i % HD for i in range(2 * HD)]


def weight_phase(nc, dram, wts, consts):
    with ExitStack() as ctx:
        sb = lambda name, shape, dt=F32: ctx.enter_context(nc.sbuf_tensor(name, shape, dt))
        sem = lambda name: ctx.enter_context(nc.semaphore(name))
        wn = sb("wn", [P, 6, C])
        bd_lat = sb("bd_lat", [P, 2, 2 * P])
        kv_bd = sb("kv_bd", [P, 2, P])
        lo_bd = sb("lo_bd", [P, 2, P])
        b_cols = sb("b_cols", [P, 6])
        lat_b = sb("lat_b", [P, 2])
        bv_rep = sb("bv_rep", [P, 2, P])
        kvb_rep = sb("kvb_rep", [P, 2, P])
        lo_b = sb("lo_b", [P, C])
        wqk_raw = sb("wqk_raw", [P, P])
        qb_raw = sb("qb_raw", [P, 1])
        vo_m = sb("vo_m", [P, P])
        lat_ps = [ctx.enter_context(nc.psum_tensor(f"lat_ps{i}", [P, HALF], F32)) for i in range(4)]
        vo_ps = [ctx.enter_context(nc.psum_tensor(f"vo_ps{i}", [P, HALF], F32)) for i in range(2)]
        m_ps = ctx.enter_context(nc.psum_tensor("m_ps", [P, HALF], F32))
        b_ps = ctx.enter_context(nc.psum_tensor("b_ps", [P, HALF], F32))
        loaded, m_done, m_copied = sem("w_loaded"), sem("m_done"), sem("m_copied")
        folded, hi_ready, split = sem("folded"), sem("w_hi_ready"), sem("w_split")
        block = ctx.enter_context(nc.Block())
        loads = [(wn, "w_nat"), (bd_lat, "bd_lat"), (kv_bd, "kv_bd"), (lo_bd, "lo_bd"), (b_cols, "b_cols"),
                 (lat_b, "lat_b"), (bv_rep, "bv_rep"), (kvb_rep, "kvb_rep"), (lo_b, "lo_b"),
                 (wqk_raw, "wqk_bd"), (qb_raw, "wqk_b"), (wts["cproj"], "cproj"), (wts["gate"], "gate"),
                 (consts["cos"], "cos"), (consts["sin"], "sin"), (consts["ident"], "ident"),
                 (consts["ident_bf"], "ident_bf"), (consts["mask"], "mask"), (consts["mask_T"], "mask_T")]

        @block.sync
        def _(sp):
            for dst, name in loads:
                sp.dma_start(dst[:], dram[name]).then_inc(loaded, 16)

        @block.tensor
        def _(pe):
            pe.wait_ge(loaded, 16 * len(loads))
            for i in range(2):
                last = nc.tensor.matmul(m_ps[:, 0:P], kv_bd[:, i, :], lo_bd[:, i, :], start=i == 0, stop=i == 1)
            last.then_inc(m_done, 1)
            for kc in range(KC):
                for side in range(2):
                    for i in range(2):
                        nc.tensor.matmul(lat_ps[2 * kc + side][:, 2 * P * i:2 * P * i + 2 * P],
                                         wn[:, 2 * side + i, P * kc:P * kc + P], bd_lat[:, side, :],
                                         start=True, stop=True)
            for side in range(2):
                for g in range(GROUPS):
                    nc.tensor.matmul(b_ps[:, GROUPS * side + g:GROUPS * side + g + 1],
                                     bd_lat[:, side, P * (g % 2):P * (g % 2) + P],
                                     b_cols[:, 2 * side + g // 2:2 * side + g // 2 + 1], start=True, stop=True)
            pe.wait_ge(m_copied, 1)
            for kc in range(KC):
                for i in range(2):
                    nc.tensor.matmul(vo_ps[kc][:, P * i:P * i + P], wn[:, 4 + i, P * kc:P * kc + P], vo_m[:],
                                     start=True, stop=True)
            for i in range(2):
                cols = slice(2 * P + P * i, 2 * P + P * i + P)
                nc.tensor.matmul(b_ps[:, cols], bv_rep[:, i, :], vo_m[:], start=True, stop=False)
                nc.tensor.matmul(b_ps[:, cols], kvb_rep[:, 0, :], lo_bd[:, 0, :], start=False, stop=False)
                last = nc.tensor.matmul(b_ps[:, cols], kvb_rep[:, 1, :], lo_bd[:, 1, :], start=False, stop=True)
            last.then_inc(folded, 1)

        @block.vector
        def _(dve):
            dve.wait_ge(m_done, 1)
            nc.vector.tensor_copy(vo_m[:], m_ps[:, 0:P]).then_inc(m_copied, 1)
            nc.vector.tensor_scalar(wts["wqk"][:], wqk_raw[:], L ** -0.5, None, ALU.mult)
            nc.vector.tensor_scalar(wts["q_bias"][:], qb_raw[:], L ** -0.5, None, ALU.mult)
            dve.wait_ge(folded, 1)
            for kc in range(KC):
                for side in range(2):
                    nc.vector.tensor_copy(wts["lat_hi"][:, kc, side, :], lat_ps[2 * kc + side][:]).then_inc(hi_ready, 1)
                nc.vector.tensor_copy(wts["vo_hi"][:, kc, :], vo_ps[kc][:, 0:C]).then_inc(hi_ready, 1)
            dve.wait_ge(hi_ready, 3 * KC)
            for kc in range(KC):
                for side in range(2):
                    nc.vector.tensor_tensor(wts["lat_lo"][:, kc, side, :], lat_ps[2 * kc + side][:],
                                            wts["lat_hi"][:, kc, side, :].bitcast(F32), ALU.subtract)
                nc.vector.tensor_tensor(wts["vo_lo"][:, kc, :], vo_ps[kc][:, 0:C],
                                        wts["vo_hi"][:, kc, :].bitcast(F32), ALU.subtract)
            for side in range(2):
                nc.vector.tensor_scalar(wts["lat_bias"][:, side, :], b_ps[:, GROUPS * side:GROUPS * side + GROUPS],
                                        lat_b[:, side:side + 1], None, ALU.add)
            nc.vector.memset(wts["eps"][:], EPS)
            nc.vector.tensor_tensor(wts["vo_bias"][:], b_ps[:, 2 * P:4 * P], lo_b[:], ALU.add).then_inc(split, 1)
            dve.wait_ge(split, 1)


def attention_phase(nc, dram, wts, consts, x1_dram, logits_dram):
    with ExitStack() as ctx:
        sb = lambda name, shape, dt=F32: ctx.enter_context(nc.sbuf_tensor(name, shape, dt))
        sem = lambda name: ctx.enter_context(nc.semaphore(name))

        x_raw = sb("x_raw", [P, T])
        x_hi = sb("x_hi", [P, KC, T], F32R)
        x_lo = sb("x_lo", [P, KC, T], F32R)
        u = [sb(f"u{s}", [P, T]) for s in range(2)]
        u_rot = sb("u_rot", [P, T])
        hi = [sb(f"qk_hi{s}", [P, T], F32R) for s in range(2)]
        q_stack = sb("q_stack", [3 * L + 2, 2, HG, T], F32R)
        k_stack = sb("k_stack", [3 * L + 2, 2, HG, T], F32R)
        v_ones = sb("v_ones", [P, 2, TB, HG, 2 * HD])
        probs = sb("probs", [P, 2, HG, 2 * HALF])
        neg_max_a = sb("neg_max_a", [P, HG * TB])
        neg_max_b = sb("neg_max_b", [P, HG * TB])
        neg_max = sb("neg_max", [P, HG * TB])
        max_hi = sb("max_hi", [HG * TB, P], F32R)
        max_lo = sb("max_lo", [HG * TB, P], F32R)
        sums = sb("sums", [P, HALF])
        y_T = sb("y_T", [P, GROUPS, T])
        z = sb("z", [P, TB, C])
        z_stats = sb("z_stats", [P, TB, 6])
        z_mv = sb("z_mv", [P, TB, 2])
        z_std = sb("z_std", [P, TB])
        z_T = x_raw[:].rearrange("p (a t) -> p a t", a=4)[:, 0:2, :]
        logits = sb("logits", [P, TB, E])
        z_rstd = sb("z_rstd", [P, TB])

        ring = [ctx.enter_context(nc.psum_tensor(f"ring{i}", [P, HALF], F32)) for i in range(2)]
        sc = [ctx.enter_context(nc.psum_tensor(f"scores_T{i}", [P, 2 * HALF], F32)) for i in range(2)]
        o_ps = [ctx.enter_context(nc.psum_tensor(f"o_ps{i}", [P, HALF], F32)) for i in range(2)]

        x_loaded, res_loaded = sem("x_loaded"), sem("res_loaded")
        x_hi_ready, x_lo_ready = sem("x_hi_ready"), sem("x_lo_ready")
        ring_full = sem("ring_full")
        begun = sem("begun")
        u_ready = [sem("u_ready_q"), sem("u_ready_k")]
        rot_loaded = [sem("rot_q"), sem("rot_k")]
        cos_done = [sem("cos_q"), sem("cos_k")]
        rope_done = [sem("rope_q_done"), sem("rope_k_done")]
        q_hi_ready, q_lo_ready = sem("q_hi_ready"), sem("q_lo_ready")
        k_hi_ready, k_lo_ready = sem("k_hi_ready"), sem("k_lo_ready")
        stacked = [sem(f"stacked{h}") for h in range(HG)]
        v_ready = sem("v_ready")
        max_taken, neg_max_ready = sem("max_taken"), sem("neg_max_ready")
        z_T_ready, logits_ready, logits_stored = sem("z_T_ready"), sem("logits_ready"), sem("logits_stored")
        sin_done = [sem("sin_q"), sem("sin_k")]
        ones_set = sem("ones_set")
        max_hi_ready, max_lo_ready, max_row = sem("max_hi_ready"), sem("max_lo_ready"), sem("max_row")
        sc_full, exp_done, pv_done = sem("sc_full"), sem("exp_done"), sem("pv_done")
        sums_read, inv_ready = sem("sums_read"), sem("inv_ready")
        o_read = sem("o_read")
        z_ready, stats_ready, mv_ready = sem("z_ready"), sem("stats_ready"), sem("mv_ready")
        std_ready, rstd_ready, x1_ready, x1_stored = (sem("std_ready"), sem("rstd_ready"), sem("x1_ready"),
                                                      sem("x1_stored"))

        def step_blocks(s):
            c, pair = STEPS[s]
            return c, [(kb, max(HALF * c, P * kb), HALF * (c + 1) - max(HALF * c, P * kb)) for kb in pair]

        def stage_a():
            return [("U", 0, 0), ("U", 0, 1), ("U", 1, 0), ("U", 1, 1)]

        def stage_s():
            return [("S", h, qb, part) for h in range(HG) for qb in range(TB) for part in range(1 + qb // 4)]

        def unit_items(scores, project, batch_in, batch_out):
            items, s_items = [], stage_s() if scores else []
            extra = {i: [] for i in range(24)}
            if project:
                for i, it in enumerate(stage_a()):
                    extra[A_FIRST + i].append(it)
            if batch_out:
                for tb in range(TB):
                    extra[5 + tb].append(("C", tb))
                extra[15].append(("NORM_Z",))
                for tb in range(TB):
                    extra[16 + tb // 2].append(("ZT", tb))
                    extra[17 + tb // 2].append(("G", tb))
            extra[14].append(("N", 0))
            for i, it in enumerate(s_items):
                extra[S_FIRST + i * (S_LAST - S_FIRST) // len(s_items)].append(it)
            if scores:
                extra[0].append(("V",))
                extra[22].append(("MT",))
            if project:
                extra[23] += [("WQ", 0), ("WQ", 1), ("ROPE_K",)]
            if batch_in:
                extra[0].append(("X",))
            for s in range(6):
                for h in range(HG):
                    items.append(("B", s, h))
                    if h == 1 and s:
                        items.append(("PV", s - 1))
                    items += extra[HG * s + h]
            return items + [("PV", 5), ("N", 1)]

        RING = {"V", "U", "WQ", "S", "MT", "C", "ZT", "G"}
        uses = lambda items: sum(it[0] in RING for it in items)
        PROLOGUE = ([("X",)] + stage_a() + [("WQ", 0), ("WQ", 1), ("ROPE_K",)],
                    stage_a() + [("WQ", 0), ("WQ", 1), ("ROPE_K",)], [("V",)] + stage_s() + [("MT",)])

        def program(emit, loop):
            r = 0
            for items, g in zip(PROLOGUE, (2, 3, 3)):
                emit(items, -1, g, (r, 0, 0))
                r += uses(items)
            head = unit_items(True, True, False, False)
            emit(head, 0, 0, (r, 0, 0))
            r += uses(head)
            body = [(unit_items(True, True, g == 2, g == 0), g) for g in (1, 2, 3, 0)]
            per = sum(uses(items) for items, _ in body)
            assert per % 2 == 0
            with loop(0, B - 1, 1) as b:
                at = r
                for items, g in body:
                    emit(items, b + 1 if g == 0 else b, g, (at, per, b))
                    at += uses(items)
            r += per * (B - 1)
            for g in (1, 2, 3):
                tail = unit_items(g < 3, g < 2, False, False)
                emit(tail, B - 1, g, (r, 0, 0))
                r += uses(tail)
            emit([("C", tb) for tb in range(TB)] + [("NORM_Z",)] + [(kind, tb) for tb in range(TB)
                                                                    for kind in ("ZT", "G")], B, 0, (r, 0, 0))

        def use(first, k):
            at, per, b = first
            return at + k + (per * b if per else 0), (at + k) % 2

        def wait_apart(eng, signal, value):
            value = value if isinstance(value, int) else eng.to_reg(value)
            eng.wait_ge(begun, 1)
            eng.wait_ge(signal, value)

        def before(b):
            return isinstance(b, int) and b < 0

        def first_group(b, g):
            return before(b) and g == 2

        def first_unit(b, g):
            return isinstance(b, int) and b == 0 and g == 0

        block = ctx.enter_context(nc.Block())

        @block.sync
        def _(sp):
            def wait(signal, value):
                wait_apart(sp, signal, value)

            def load_x(b, kc):
                sp.dma_start(x_raw[:], dram["xT"][b, P * kc:P * kc + P, :]).then_inc(x_loaded, 16)

            def load_residual(b):
                sp.dma_start(z[:], dram["x"][b].rearrange("(tb p) c -> p tb c", p=P)).then_inc(res_loaded, 16)

            def swap_rows(m):
                for s in range(2):
                    wait(u_ready[s], 2 * m + 2)
                    if s == 1:
                        wait(rope_done[0], m + 1)
                    sp.dma_start(u_rot[0:P:2, :], u[s][1:P:2, :]).then_inc(rot_loaded[s], 16)
                    sp.dma_start(u_rot[1:P:2, :], u[s][0:P:2, :]).then_inc(rot_loaded[s], 16)

            def stack(m, par, first):
                wait(q_lo_ready, 2 * m + 2)
                wait(k_lo_ready, m + 1)
                if not first:
                    wait(sc_full, 24 * (m - 1))
                for h in range(HG):
                    rows = slice(L * h, L * h + L)
                    for stk, i, src in ((q_stack, 0, hi[0]), (q_stack, 1, hi[0]), (q_stack, 2, u[0]),
                                        (k_stack, 0, hi[1]), (k_stack, 1, u[1]), (k_stack, 2, hi[1])):
                        sp.dma_start(stk[L * i:L * i + L, par, h, :].bitcast(F32),
                                     src[rows, :].bitcast(F32)).then_inc(stacked[h], 16)

            def max_rows(m, par):
                wait(max_lo_ready, m + 1)
                for row, src in ((3 * L, max_hi), (3 * L + 1, max_lo)):
                    sp.dma_start(q_stack[row:row + 1, par, :, :].bitcast(F32), src[:].bitcast(F32)).then_inc(max_row, 16)

            def store(b):
                wait(x1_ready, TB * b + TB)
                sp.dma_start(x1_dram[b].rearrange("(tb p) c -> p tb c", p=P), z[:]).then_inc(x1_stored, 16)

            def store_logits(b):
                wait(logits_ready, TB * b + TB)
                sp.dma_start(logits_dram[b].rearrange("tb p e -> p tb e"), logits[:]).then_inc(logits_stored, 16)

            load_x(0, 0)
            load_residual(0)
            wait(x_lo_ready, 1)
            load_x(0, 1)
            swap_rows(0)
            stack(0, 0, True)
            swap_rows(1)
            max_rows(0, 0)
            stack(1, 1, True)
            swap_rows(2)
            max_rows(1, 1)
            with sp.Fori(0, B - 1, 1) as b:
                for g in (1, 2, 3, 0):
                    n = 4 * b + (g or 4)
                    stack(n + 1, (g + 1) % 2, False)
                    if g in (1, 2):
                        wait(x_lo_ready, 2 * b + g + 1)
                        load_x(b + 1, g - 1)
                    swap_rows(n + 2)
                    if g == 0:
                        store(b)
                        wait(x1_stored, 16 * b + 16)
                        store_logits(b)
                        wait(logits_stored, 16 * b + 16)
                        load_residual(b + 1)
                    max_rows(n + 1, (g + 1) % 2)
            for g in (1, 2, 3):
                n = 4 * (B - 1) + g
                if g < 3:
                    stack(n + 1, (g + 1) % 2, False)
                if g < 2:
                    swap_rows(n + 2)
                if g < 3:
                    max_rows(n + 1, (g + 1) % 2)
            store(B - 1)
            store_logits(B - 1)
            wait(x1_stored, 16 * B)
            wait(logits_stored, 16 * B)

        @block.tensor
        def _(pe):
            recent = []

            def read_by(it, n, b):
                kind = it[0]
                if kind == "V":
                    return v_ready, n + 2
                if kind == "U":
                    return u_ready[it[1]], 2 * (n + 2) + it[2] + 1
                if kind == "WQ":
                    return q_lo_ready, 2 * (n + 2) + it[1] + 1
                if kind == "S":
                    return max_taken, 48 * (n + 1) + stage_s().index(it) + 1
                if kind == "MT":
                    return max_lo_ready, n + 2
                signal = {"C": z_ready, "ZT": z_T_ready, "G": logits_ready}[kind]
                return signal, TB * (b - 1) + it[1] + 1

            def emit(items, b, g, first):
                n = 4 * b + g
                k = 0
                if first[1] and g == 1:
                    recent[:] = [read_by(("WQ", 0), n - 1, b), read_by(("WQ", 1), n - 1, b)]
                for it in items:
                    kind = it[0]
                    if kind in RING:
                        number, slot = use(first, k)
                        k += 1
                        if len(recent) == 2:
                            pe.wait_ge(*recent.pop(0))
                        recent.append(read_by(it, n, b))
                        out = ring[slot]
                    if kind == "B":
                        s, h = it[1:]
                        t = 24 * n + HG * s + h
                        if s == 0 and h == 0:
                            pe.wait_ge(max_row, 32 * n + 32)
                            if first_unit(b, g):
                                pe.wait_ge(ones_set, 1)
                        if not (first_unit(b, g) and HG * s + h < 2):
                            pe.wait_ge(exp_done, t - 1)
                        c, blocks = step_blocks(s)
                        dst = sc[(HG * s + h) % 2]
                        for j, (kb, q0, w) in enumerate(blocks):
                            cols = slice(HALF - w, HALF) if j == 0 else slice(HALF, HALF + w)
                            diag = P * kb >= HALF * c
                            last = nc.tensor.matmul(dst[:, cols], k_stack[:, g % 2, h, P * kb:P * kb + P],
                                                    q_stack[:, g % 2, h, q0:q0 + w], start=True, stop=not diag)
                            if diag:
                                last = nc.tensor.matmul(dst[:, cols.start:cols.start + P], consts["ident_bf"][:],
                                                        consts["mask_T"][:], start=False, stop=True)
                        last.then_inc(sc_full, 1)
                    elif kind == "PV":
                        s = it[1]
                        c, blocks = step_blocks(s)
                        pe.wait_ge(exp_done, 24 * n + HG * s + HG)
                        if s == 0:
                            pe.wait_ge(v_ready, n + 1)
                        if s in (0, 2) and not first_unit(b, g):
                            pe.wait_ge(o_read, 2 * n - 1 + c)
                        for j, (kb, q0, w) in enumerate(blocks):
                            cols = slice(HALF - w, HALF) if j == 0 else slice(HALF, HALF + w)
                            for h in range(HG):
                                last = nc.tensor.matmul(o_ps[c][32 * h:32 * h + 32, q0 - HALF * c:HALF],
                                                        v_ones[:, g % 2, kb, h, :], probs[:, s % 2, h, cols],
                                                        start=kb == 0, stop=kb == 4 * c + 3)
                        last.then_inc(pv_done, 1)
                    elif kind == "V":
                        gm = (g + 1) % 4
                        for tb in range(TB):
                            t = slice(P * tb, P * tb + P)
                            terms = [(a, w_, kc) for kc in range(KC) for a, w_ in
                                     ((x_hi, wts["vo_hi"]), (x_hi, wts["vo_lo"]), (x_lo, wts["vo_hi"]))]
                            for i, (a, w_, kc) in enumerate(terms):
                                last = nc.tensor.matmul(out[:, 64 * tb:64 * tb + 64], a[:, kc, t],
                                                        w_[:, kc, 64 * gm:64 * gm + 64], start=i == 0, stop=i == 5)
                        last.then_inc(ring_full, 1)
                    elif kind == "U":
                        side, half = it[1:]
                        gm = (g + 2) % 4
                        if gm == 0 and side == 0 and half == 0:
                            pe.wait_ge(x_lo_ready, 2 * b + 4)
                        cols = slice(HALF * half, HALF * half + HALF)
                        m_cols = slice(P * gm, P * gm + P)
                        terms = [(w_, a, kc) for kc in range(KC) for w_, a in
                                 ((wts["lat_hi"], x_hi), (wts["lat_hi"], x_lo), (wts["lat_lo"], x_hi))]
                        for i, (w_, a, kc) in enumerate(terms):
                            last = nc.tensor.matmul(out[:], w_[:, kc, side, m_cols], a[:, kc, cols],
                                                    start=i == 0, stop=i == 5)
                        last.then_inc(ring_full, 1)
                    elif kind == "WQ":
                        half = it[1]
                        if half == 0:
                            pe.wait_ge(rope_done[0], n + 3)
                        nc.tensor.matmul(out[:], wts["wqk"][:], u[0][:, HALF * half:HALF * half + HALF],
                                         start=True, stop=True).then_inc(ring_full, 1)
                    elif kind == "S":
                        h, qb, part = it[1:]
                        par = (g + 1) % 2
                        if qb == 0:
                            pe.wait_ge(stacked[h], 96 * (n + 2))
                        k0, k1 = HALF * part, min(HALF * part + HALF, P * (qb + 1))
                        diag = k1 == P * (qb + 1)
                        last = nc.tensor.matmul(out[:, 0:k1 - k0], q_stack[0:3 * L, par, h, P * qb:P * qb + P],
                                                k_stack[0:3 * L, par, h, k0:k1], start=True, stop=not diag)
                        if diag:
                            last = nc.tensor.matmul(out[:, k1 - k0 - P:k1 - k0], consts["ident_bf"][:],
                                                    consts["mask"][:], start=False, stop=True)
                        last.then_inc(ring_full, 1)
                    elif kind == "MT":
                        pe.wait_ge(neg_max_ready, n + 2)
                        nc.tensor.transpose(out[0:HG * TB, 0:P], neg_max[:], consts["ident"][:]).then_inc(ring_full, 1)
                    elif kind == "C":
                        tb = it[1]
                        if tb == 0:
                            pe.wait_ge(o_read, 8 * b)
                        for gy in range(GROUPS):
                            last = nc.tensor.matmul(out[:, 0:C], y_T[:, gy, P * tb:P * tb + P], wts["cproj"][:, gy, :],
                                                    start=gy == 0, stop=gy == GROUPS - 1)
                        last.then_inc(ring_full, 1)

                    elif kind == "ZT":
                        tb = it[1]
                        if tb == 0:
                            pe.wait_ge(x1_ready, TB * b)
                        for kc in range(KC):
                            last = nc.tensor.transpose(out[:, P * kc:P * kc + P], z[:, tb, P * kc:P * kc + P],
                                                       consts["ident"][:])
                        last.then_inc(ring_full, 1)
                    elif kind == "G":
                        tb = it[1]
                        pe.wait_ge(z_T_ready, TB * (b - 1) + tb + 1)
                        for kc in range(KC):
                            last = nc.tensor.matmul(out[:, 0:E], z_T[:, tb % 2, P * kc:P * kc + P],
                                                    wts["gate"][:, kc, :], start=kc == 0, stop=kc == KC - 1)
                        last.then_inc(ring_full, 1)

            program(emit, pe.Fori)

        @block.scalar
        def _(act):
            def emit(items, b, g, first):
                n = 4 * b + g
                gm = (g + 2) % 4
                k = 0
                for it in items:
                    kind = it[0]
                    if kind in RING:
                        number, slot = use(first, k)
                        k += 1
                        src = ring[slot]
                    if kind == "B":
                        s, h = it[1:]
                        c, blocks = step_blocks(s)
                        cols = slice(HALF - blocks[0][2], HALF + blocks[1][2])
                        act.wait_ge(sc_full, 24 * n + HG * s + h + 1)
                        if h == 0 and not (first_unit(b, g) and s < 2):
                            act.wait_ge(pv_done, 6 * n + s - 1)
                        nc.scalar.activation(probs[:, s % 2, h, cols], sc[(HG * s + h) % 2][:, cols],
                                             ACT.Exp).then_inc(exp_done, 1)
                    elif kind == "U":
                        side, half = it[1:]
                        act.wait_ge(ring_full, number + 1)
                        if half == 0 and side == 0 and not first_group(b, g):
                            for h in range(HG):
                                act.wait_ge(stacked[h], 96 * (n + 2))
                        nc.scalar.activation(u[side][:, HALF * half:HALF * half + HALF], src[:], ACT.Identity,
                                             bias=wts["lat_bias"][:, side, gm:gm + 1]).then_inc(u_ready[side], 1)
                    elif kind == "ROPE_K":
                        act.wait_ge(rope_done[1], n + 3)
                        nc.scalar.activation(hi[1][:], u[1][:], ACT.Identity).then_inc(k_hi_ready, 1)
                    elif kind == "WQ":
                        cols = slice(HALF * it[1], HALF * it[1] + HALF)
                        act.wait_ge(ring_full, number + 1)
                        nc.scalar.activation(hi[0][:, cols], src[:], ACT.Identity,
                                             bias=wts["q_bias"][:, 0:1]).then_inc(q_hi_ready, 1)
                    elif kind == "MT":
                        act.wait_ge(ring_full, number + 1)
                        if not before(b):
                            act.wait_ge(max_row, 32 * (n + 1))
                        nc.scalar.activation(max_hi[:], src[0:HG * TB, 0:P], ACT.Identity).then_inc(max_hi_ready, 1)
                    elif kind == "NORM_Z":
                        act.wait_ge(mv_ready, TB * b)
                        nc.scalar.activation(z_std[:], z_mv[:, :, 1], ACT.Sqrt,
                                             bias=wts["eps"][:, 0:1]).then_inc(std_ready, 1)

            program(emit, act.Fori)

        @block.vector
        def _(dve):
            def emit(items, b, g, first):
                n = 4 * b + g
                gm = (g + 2) % 4
                k = 0
                for it in items:
                    kind = it[0]
                    if kind in RING:
                        number, slot = use(first, k)
                        k += 1
                        src = ring[slot]
                        if kind != "U":
                            if kind == "MT":
                                dve.wait_ge(max_taken, 48 * (n + 2))
                                nc.vector.tensor_tensor(neg_max[:], neg_max_a[:], neg_max_b[:],
                                                        ALU.min).then_inc(neg_max_ready, 1)
                            dve.wait_ge(ring_full, number + 1)
                    if kind == "X":
                        for kc in range(KC):
                            dve.wait_ge(x_loaded, 16 * (2 * b + kc + 3))
                            nc.vector.tensor_copy(x_hi[:, kc, :], x_raw[:]).then_inc(x_hi_ready, 1)
                            dve.wait_ge(x_hi_ready, 2 * b + kc + 3)
                            nc.vector.tensor_tensor(x_lo[:, kc, :], x_raw[:], x_hi[:, kc, :].bitcast(F32),
                                                    ALU.subtract).then_inc(x_lo_ready, 1)
                    elif kind == "V":
                        gv = (g + 1) % 4
                        bias = wts["vo_bias"][:, 64 * gv:64 * gv + 64].rearrange("p (h d) -> p h d", h=HG)
                        nc.vector.tensor_tensor(v_ones[:, gv % 2, :, :, 0:HD],
                                                src[:].rearrange("p (t h d) -> p t h d", t=TB, h=HG),
                                                bias.unsqueeze(1).to_broadcast([P, TB, HG, HD]),
                                                ALU.add).then_inc(v_ready, 1)
                    elif kind == "ROPE_K":
                        dve.wait_ge(k_hi_ready, n + 3)
                        nc.vector.tensor_tensor(u[1][:].bitcast(F32R), u[1][:], hi[1][:].bitcast(F32),
                                                ALU.subtract).then_inc(k_lo_ready, 1)
                    elif kind == "WQ":
                        cols = slice(HALF * it[1], HALF * it[1] + HALF)
                        dve.wait_ge(q_hi_ready, 2 * (n + 2) + it[1] + 1)
                        nc.vector.scalar_tensor_tensor(out=u[0][:, cols].bitcast(F32R), in0=src[:], scalar=wts["q_bias"][:, 0:1],
                                                       in1=hi[0][:, cols].bitcast(F32), op0=ALU.add,
                                                       op1=ALU.subtract).then_inc(q_lo_ready, 1)
                    elif kind == "S":
                        h, qb, part = it[1:]
                        w = min(HALF * part + HALF, P * (qb + 1)) - HALF * part
                        dst = (neg_max_a, neg_max_b)[part]
                        nc.vector.tensor_reduce(dst[:, TB * h + qb:TB * h + qb + 1], src[:, 0:w], AX_X, ALU.max,
                                                negate=True).then_inc(max_taken, 1)
                    elif kind == "MT":
                        dve.wait_ge(max_hi_ready, n + 2)
                        nc.vector.tensor_tensor(max_lo[:], src[0:HG * TB, 0:P], max_hi[:].bitcast(F32),
                                                ALU.subtract).then_inc(max_lo_ready, 1)
                    elif kind == "N":
                        c = it[1]
                        cols = slice(HALF * c, HALF * c + HALF)
                        if not (first_unit(b, g) and c == 0):
                            dve.wait_ge(o_read, 2 * n + c)
                        wait_apart(dve, pv_done, 6 * n + (2, 6)[c])
                        nc.vector.stream_shuffle(sums[:], o_ps[c][:], SUM_ROWS).then_inc(sums_read, 1)
                        dve.wait_ge(sums_read, 2 * n + c + 1)
                        nc.vector.reciprocal(sums[:], sums[:]).then_inc(inv_ready, 1)
                        dve.wait_ge(inv_ready, 2 * n + c + 1)
                        nc.vector.tensor_tensor(y_T[:, g, cols], o_ps[c][:], sums[:],
                                                ALU.mult).then_inc(o_read, 1)
                    elif kind == "C":
                        tb = it[1]
                        done = TB * (b - 1) + tb + 1
                        if tb == 0:
                            dve.wait_ge(res_loaded, 16 * b)
                        nc.vector.tensor_tensor(z[:, tb, :], src[:, 0:C], z[:, tb, :], ALU.add).then_inc(z_ready, 1)
                        dve.wait_ge(z_ready, done)
                        nc.vector.bn_stats(z_stats[:, tb, :], z[:, tb, :]).then_inc(stats_ready, 1)
                        wait_apart(dve, stats_ready, done)
                        nc.vector.bn_aggr(z_mv[:, tb, :], z_stats[:, tb, :]).then_inc(mv_ready, 1)
                    elif kind == "ZT":
                        nc.vector.tensor_copy(z_T[:, it[1] % 2, :], src[:, 0:C]).then_inc(z_T_ready, 1)
                    elif kind == "G":
                        nc.vector.tensor_copy(logits[:, it[1], :], src[:, 0:E]).then_inc(logits_ready, 1)
                    elif kind == "NORM_Z":
                        dve.wait_ge(std_ready, b)
                        nc.vector.reciprocal(z_rstd[:], z_std[:]).then_inc(rstd_ready, 1)
                        dve.wait_ge(rstd_ready, b)
                        for tb in range(TB):
                            nc.vector.tensor_scalar(z[:, tb, :], z[:, tb, :], z_mv[:, tb, 0:1], z_rstd[:, tb:tb + 1],
                                                    ALU.subtract, ALU.mult).then_inc(x1_ready, 1)

            nc.vector.memset(v_ones[:], 1.0)
            nc.vector.memset(neg_max_b[:], -NEG).then_inc(begun, 1)
            program(emit, dve.Fori)

        @block.gpsimd
        def _(pool):
            def rotate(m, s):
                pool.wait_ge(rot_loaded[s], 32 * m + 32)
                nc.gpsimd.tensor_tensor(u[s][:], u[s][:], consts["cos"][:], ALU.mult).then_inc(cos_done[s], 1)
                nc.gpsimd.tensor_tensor(u_rot[:], u_rot[:], consts["sin"][:], ALU.mult).then_inc(sin_done[s], 1)
                pool.wait_ge(cos_done[s], m + 1)
                pool.wait_ge(sin_done[s], m + 1)
                nc.gpsimd.tensor_tensor(u[s][:], u[s][:], u_rot[:], ALU.add).then_inc(rope_done[s], 1)

            nc.gpsimd.memset(k_stack[3 * L:3 * L + 2, :, :, :].bitcast(F32), 1.0).then_inc(ones_set, 1)
            pool.wait_ge(ones_set, 1)
            with pool.Fori(0, GROUPS * B, 1) as m:
                for s in range(2):
                    rotate(m, s)


def routing_phase(nc, dram, logits_dram, experts, routes, token_of_slot):
    with ExitStack() as ctx:
        sb = lambda name, shape, dt=F32: ctx.enter_context(nc.sbuf_tensor(name, shape, dt))
        sem = lambda name: ctx.enter_context(nc.semaphore(name))
        full = [P, TILES, E]
        logits = sb("all_logits", full)
        logits_loaded = sem("logits_loaded")
        rank = sb("rank", [P, E])
        limit = sb("limit", [P, TILES])
        slot_no = sb("slot_no", [P, MAX_TILES])
        ids = sb("ids", [P, TILES], I32)
        before = sb("before", [P, P], BF16)
        ones = sb("ones_bf", [P, P], BF16)
        top = [sb(f"top{k}", [P, TILES]) for k in range(2)]
        pick = [sb(f"pick{k}", full) for k in range(2)]
        rest = sb("rest", full)
        tmp = sb("route_tmp", full)
        tmp1 = sb("route_tmp1", [P, TILES])
        chosen = sb("chosen", full, BF16)
        run = [sb(f"run{k}", full) for k in range(2)]
        pos = sb("pos", full)
        over = sb("over", [P, E, TILES])
        tiles = [sb(f"tiles{k}", [P, E]) for k in range(2)]
        base = sb("base", [P, E])
        past = sb("past", [P, MAX_TILES, E])
        expert_f = sb("expert_f", [P, MAX_TILES])
        zero_ids = sb("zero_ids", [P, MAX_TILES], I32)
        tok_rows = sb("tok_rows", [HALF_TILES, 2, P], I32)
        tok_f = sb("tok_f", [HALF_TILES, 2, P])
        within_ps = ctx.enter_context(nc.psum_tensor("within_ps", [P, HALF], F32))
        count_ps = ctx.enter_context(nc.psum_tensor("count_ps", [P, HALF], F32))
        tok_ps = ctx.enter_context(nc.psum_tensor("tok_ps", [P, HALF], F32))
        tables, b_loaded, experts_loaded = sem("tables"), sem("b_loaded"), sem("experts_loaded")
        step, counted = sem("route_step"), sem("counted")
        diff_ready, exp_ready, pos_ready = sem("diff_ready"), sem("exp_ready"), sem("pos_ready")
        zero_set, zeroed, scattered, tok_loaded = (sem("zero_set"), sem("zeroed"), sem("scattered"),
                                                   sem("tok_loaded"))
        tok_f_ready, tok_turned, done = sem("tok_f_ready"), sem("tok_turned"), sem("route_done")
        table_loads = [(rank, "rank"), (limit, "limit"), (slot_no, "slot_no"), (ids, "ids"), (before, "before"),
                       (ones, "ones")]
        b_raw = sb("b_raw", [2, E, H + C])
        block = ctx.enter_context(nc.Block())

        @block.sync
        def _(sp):
            for dst, name in table_loads:
                sp.dma_start(dst[:], dram[name]).then_inc(tables, 16)
            sp.dma_start(logits[:], logits_dram.rearrange("b t p e -> p (b t) e")).then_inc(logits_loaded, 16)
            sp.dma_start(b_raw[:], dram["b12"]).then_inc(b_loaded, 16)
            sp.dma_start(routes["split"][:], dram["split"]).then_inc(b_loaded, 16)
            for name in EXPERT_LOADS:
                sp.dma_start(experts[name][:], dram[name]).then_inc(experts_loaded, 16)
            sp.wait_ge(zero_set, 1)
            sp.dma_start(token_of_slot.rearrange("(p s) o -> p (s o)", p=P), zero_ids[:]).then_inc(zeroed, 16)
            sp.wait_ge(scattered, 16 * 2 * TILES)
            sp.dma_start(tok_rows[:], token_of_slot.rearrange("(a s p) o -> s a (p o)", a=2, p=P)).then_inc(
                tok_loaded, 16)
            sp.wait_ge(experts_loaded, 16 * len(EXPERT_LOADS))

        @block.tensor
        def _(pe):
            pe.wait_ge(tables, 16 * len(table_loads))
            pe.wait_ge(pos_ready, 1)
            flat = chosen[:].rearrange("p t e -> p (t e)")
            nc.tensor.matmul(within_ps[:], before[:], flat, start=True, stop=True)
            nc.tensor.matmul(count_ps[:], ones[:], flat, start=True, stop=True).then_inc(counted, 1)
            pe.wait_ge(tok_f_ready, 1)
            for a in range(2):
                last = nc.tensor.transpose(tok_ps[:, HALF_TILES * a:HALF_TILES * (a + 1)], tok_f[:, a, :],
                                           routes["ident"][0:HALF_TILES, 0:HALF_TILES])
            last.then_inc(tok_turned, 1)

        @block.scalar
        def _(act):
            act.wait_ge(diff_ready, 1)
            nc.scalar.activation(tmp1[:], tmp1[:], ACT.Exp).then_inc(exp_ready, 1)

        @block.gpsimd
        def _(pool):
            nc.gpsimd.memset(zero_ids[:], 0).then_inc(zero_set, 1)
            pool.wait_ge(zeroed, 16)
            pool.wait_ge(tables, 16 * len(table_loads))
            pool.wait_ge(pos_ready, 2)
            for k in range(2):
                for j in range(TILES):
                    nc.gpsimd.indirect_dma_start(
                        token_of_slot, bass.IndirectOffsetOnAxis(routes["slot"][:, k, j:j + 1], 0),
                        ids[:, j:j + 1], None).then_inc(scattered, 16)

        @block.vector
        def _(dve):
            steps = [0]

            def then(ins):
                steps[0] += 1
                ins.then_inc(step, 1)
                dve.wait_ge(step, steps[0])

            def over_tiles(a):
                return a[:].unsqueeze(2).to_broadcast(full)

            dve.wait_ge(tables, 16 * len(table_loads))
            dve.wait_ge(logits_loaded, 16)
            for k in range(2):
                src = (logits, rest)[k]
                then(nc.vector.tensor_reduce(top[k][:], src[:], AX_X, ALU.max))
                then(nc.vector.tensor_tensor(tmp[:], src[:], over_tiles(top[k]), ALU.is_equal))
                then(nc.vector.tensor_tensor(tmp[:], tmp[:], rank[:].unsqueeze(1).to_broadcast(full), ALU.mult))
                then(nc.vector.tensor_reduce(tmp1[:], tmp[:], AX_X, ALU.max))
                then(nc.vector.tensor_tensor(pick[k][:], tmp[:], over_tiles(tmp1), ALU.is_equal))
                if k == 0:
                    then(nc.vector.scalar_tensor_tensor(
                        out=rest[:].rearrange("p t e -> p (t e)"), in0=pick[0][:].rearrange("p t e -> p (t e)"),
                        scalar=NEG, in1=logits[:].rearrange("p t e -> p (t e)"), op0=ALU.mult, op1=ALU.add))
            then(nc.vector.tensor_tensor(chosen[:], pick[0][:], pick[1][:], ALU.add))
            nc.vector.tensor_tensor(tmp1[:], top[1][:], top[0][:], ALU.subtract).then_inc(diff_ready, 1)
            dve.wait_ge(exp_ready, 1)
            then(nc.vector.tensor_scalar(top[0][:], tmp1[:], 1.0, None, ALU.add))
            then(nc.vector.reciprocal(routes["weight"][:, 0, :], top[0][:]))
            nc.vector.tensor_tensor(routes["weight"][:, 1, :], routes["weight"][:, 0, :], tmp1[:],
                                    ALU.mult).then_inc(pos_ready, 1)
            dve.wait_ge(counted, 1)
            counts = count_ps[:].rearrange("p (t e) -> p t e", e=E)
            then(nc.vector.tensor_copy(run[0][:], counts))
            cur, s = 0, 1
            while s < TILES:
                then(nc.vector.tensor_copy(run[1 - cur][:, 0:s, :], run[cur][:, 0:s, :]))
                then(nc.vector.tensor_tensor(run[1 - cur][:, s:, :], run[cur][:, s:, :], run[cur][:, 0:TILES - s, :],
                                             ALU.add))
                cur, s = 1 - cur, 2 * s
            total = run[cur][:, TILES - 1, :]
            then(nc.vector.tensor_tensor(over[:], total.unsqueeze(2).to_broadcast([P, E, TILES]),
                                         limit[:].unsqueeze(1).to_broadcast([P, E, TILES]), ALU.is_gt))
            then(nc.vector.tensor_reduce(tiles[0][:], over[:], AX_X, ALU.add))
            then(nc.vector.tensor_copy(base[:], tiles[0][:]))
            at, s = 0, 1
            while s < E:
                then(nc.vector.tensor_copy(tiles[1 - at][:, 0:s], tiles[at][:, 0:s]))
                then(nc.vector.tensor_tensor(tiles[1 - at][:, s:], tiles[at][:, s:], tiles[at][:, 0:E - s], ALU.add))
                at, s = 1 - at, 2 * s
            ends = tiles[at]
            then(nc.vector.tensor_tensor(base[:], ends[:], base[:], ALU.subtract))
            then(nc.vector.tensor_scalar(base[:], base[:], float(P), None, ALU.mult))
            then(nc.vector.tensor_tensor(past[:], slot_no[:].unsqueeze(2).to_broadcast([P, MAX_TILES, E]),
                                         ends[:].unsqueeze(1).to_broadcast([P, MAX_TILES, E]), ALU.is_ge))
            then(nc.vector.tensor_reduce(expert_f[:], past[:], AX_X, ALU.add))
            then(nc.vector.tensor_scalar(expert_f[:], expert_f[:], float(E - 1), None, ALU.min))
            then(nc.vector.tensor_copy(routes["expert"][:], expert_f[0:1, :]))
            then(nc.vector.tensor_tensor(run[cur][:], run[cur][:], counts, ALU.subtract))
            then(nc.vector.tensor_tensor(pos[:], run[cur][:], within_ps[:].rearrange("p (t e) -> p t e", e=E), ALU.add))
            then(nc.vector.tensor_tensor(pos[:], pos[:], base[:].unsqueeze(1).to_broadcast(full), ALU.add))
            for k in range(2):
                then(nc.vector.tensor_tensor(tmp[:], pos[:], pick[k][:], ALU.mult))
                then(nc.vector.tensor_reduce(top[k][:], tmp[:], AX_X, ALU.add))
            nc.vector.tensor_copy(routes["slot"][:, 0, :], top[0][:])
            nc.vector.tensor_copy(routes["slot"][:, 1, :], top[1][:]).then_inc(pos_ready, 1)
            nc.vector.tensor_copy(routes["ones2"][:], ones[0:2, :])
            dve.wait_ge(b_loaded, 32)
            for dst, cols in ((experts["b1"], slice(0, H)), (experts["b2"], slice(H, H + C))):
                then(nc.vector.tensor_copy(dst[:], b_raw[:, :, cols]))
                then(nc.vector.tensor_tensor(b_raw[:, :, cols], b_raw[:, :, cols], dst[:].bitcast(F32), ALU.subtract))
                then(nc.vector.tensor_scalar(b_raw[:, :, cols], b_raw[:, :, cols], routes["split"][:, 1:2], None,
                                             ALU.mult))
                for e in range(E):
                    then(nc.vector.scalar_tensor_tensor(out=dst[:, e, :], in0=dst[:, e, :].bitcast(F32),
                                                        scalar=routes["split"][:, 0:1], in1=b_raw[:, e, cols],
                                                        op0=ALU.mult, op1=ALU.add))
            dve.wait_ge(tok_loaded, 16)
            nc.vector.tensor_copy(tok_f[:], tok_rows[:]).then_inc(tok_f_ready, 1)
            dve.wait_ge(tok_turned, 1)
            nc.vector.tensor_copy(routes["token"][:], tok_ps[:, 0:MAX_TILES].rearrange("p (a s) -> p a s", a=2)
                                  ).then_inc(done, 1)
            dve.wait_ge(done, 1)


def expert_phase(nc, experts, routes, x1_rows, y_rows):
    with ExitStack() as ctx:
        sb = lambda name, shape, dt=F32: ctx.enter_context(nc.sbuf_tensor(name, shape, dt))
        sem = lambda name: ctx.enter_context(nc.semaphore(name))
        tok = [sb(f"tok{a}", [P, 1], I32) for a in range(2)]
        x_in = [sb(f"x_in{a}", [P, C]) for a in range(2)]
        x_T = [sb(f"x_T{a}", [P, KC, P]) for a in range(2)]
        h_stats = [sb(f"h_stats{a}", [P, 6]) for a in range(2)]
        h_mv = [sb(f"h_mv{a}", [P, 2]) for a in range(2)]
        h_ve = [sb(f"h_ve{a}", [P, 1]) for a in range(2)]
        h_rstd = [sb(f"h_rstd{a}", [P, 1]) for a in range(2)]
        h_norm = [sb(f"h_norm{a}", [P, H]) for a in range(2)]
        g_T = [sb(f"g_T{a}", [P, FC, P]) for a in range(2)]
        y_out = [sb(f"y_out{a}", [P, C]) for a in range(2)]
        ps = lambda name: [ctx.enter_context(nc.psum_tensor(f"{name}{a}", [P, HALF], F32)) for a in range(2)]
        xt_ps, h_ps, ht_ps, y_ps = ps("xt_ps"), ps("h_ps"), ps("ht_ps"), ps("y_ps")
        tok_ready = sem("tok_ready")
        x_in_loaded = [sem("x_in_loaded0"), sem("x_in_loaded1")]
        xt_full, x_T_ready, h_full, stats_done, mv_done = (sem("xt_full"), sem("x_T_ready"), sem("h_full"),
                                                           sem("h_stats_done"), sem("h_mv_done"))
        ve_done, rstd_done, h_norm_ready, ht_full = (sem("h_ve_done"), sem("h_rstd_done"), sem("h_norm_ready"),
                                                     sem("ht_full"))
        g_ready, y_full, y_ready, begun = sem("g_ready"), sem("y_full"), sem("y_ready"), sem("expert_begun")
        y_stored = [sem("y_stored0"), sem("y_stored1")]

        block = ctx.enter_context(nc.Block())

        def wait_apart(eng, signal, value):
            value = value if isinstance(value, int) else eng.to_reg(value)
            eng.wait_ge(begun, 1)
            eng.wait_ge(signal, value)

        def walk(step, eng, first, last):
            lo, hi = 4, MAX_TILES - 4
            for k in range(first, lo):
                step(k, k // 2, k % 2)
            with eng.Fori(lo // 2, hi // 2, 1) as i:
                for a in range(2):
                    step(2 * i + a, i, a)
            for k in range(hi, last):
                step(k, k // 2, k % 2)

        def within(k, n=0):
            return not isinstance(k, int) or 0 <= k < MAX_TILES

        def above(k, n):
            return not isinstance(k, int) or k >= n

        @block.gpsimd
        def _(pool):
            def step(k, i, a):
                if within(k + 3):
                    j, ja, ji = k + 3, (a + 1) % 2, (i + 2 if a else i + 1)
                    if above(j, 2):
                        pool.wait_ge(xt_full, j - 1)
                        wait_apart(pool, x_in_loaded[ja], 16 * ji)
                    nc.gpsimd.tensor_copy(tok[ja][:], routes["token"][:, ja, bass.ds(ji, 1)]).then_inc(tok_ready, 1)
                    wait_apart(pool, tok_ready, j + 1)
                    nc.gpsimd.indirect_dma_start(x_in[ja][:], None, x1_rows,
                                                 bass.IndirectOffsetOnAxis(tok[ja][:, 0:1], 0)
                                                 ).then_inc(x_in_loaded[ja], 16)
                if within(k + 1):
                    j, ja = k + 1, 1 - a
                    pool.wait_ge(ve_done, j + 1)
                    nc.gpsimd.tensor_tensor(h_rstd[ja][:], h_ve[ja][:], routes["minus_half"][:],
                                            ALU.pow).then_inc(rstd_done, 1)
            walk(step, pool, -3, MAX_TILES)

        @block.sync
        def _(sp):
            def step(k, i, a):
                if within(k):
                    wait_apart(sp, y_ready, k + 1)
                    row = P * HALF_TILES * a + P * i
                    sp.dma_start(y_rows[bass.ds(row, P), :], y_out[a][:]).then_inc(y_stored[a], 16)
            walk(step, sp, 0, MAX_TILES)
            for a in range(2):
                sp.wait_ge(y_stored[a], 16 * HALF_TILES)

        @block.tensor
        def _(pe):
            def expert(j, ja, ji):
                return pe.value_load(routes["expert"][0:1, bass.ds(HALF_TILES * ja + ji, 1)], min_val=0, max_val=E - 1)

            def step(k, i, a):
                if within(k + 2):
                    j, ja = k + 2, a
                    pe.wait_ge(x_in_loaded[ja], 16 * (i + 2))
                    if above(j, 2):
                        pe.wait_ge(x_T_ready, j - 1)
                    for kc in range(KC):
                        last = nc.tensor.transpose(xt_ps[ja][:, P * kc:P * kc + P], x_in[ja][:, P * kc:P * kc + P],
                                                   routes["ident"][:])
                    last.then_inc(xt_full, 1)
                if within(k + 1):
                    j, ja, ji = k + 1, 1 - a, (i + 1 if a else i)
                    e = expert(j, ja, ji)
                    pe.wait_ge(x_T_ready, j + 1)
                    if above(j, 2):
                        pe.wait_ge(h_norm_ready, j - 1)
                    for kc in range(KC):
                        nc.tensor.matmul(h_ps[ja][:], x_T[ja][:, kc, :], experts["w1"][:, kc, bass.ds(e, 1), :],
                                         start=kc == 0, stop=False)
                    nc.tensor.matmul(h_ps[ja][:], routes["ones2"][:], experts["b1"][:, bass.ds(e, 1), :],
                                     start=False, stop=True).then_inc(h_full, 1)
                if within(k):
                    pe.wait_ge(h_norm_ready, k + 1)
                    if above(k, 2):
                        pe.wait_ge(g_ready, FC * (k - 1))
                    for f in range(FC):
                        last = nc.tensor.transpose(ht_ps[a][:, P * f:P * f + P], h_norm[a][:, P * f:P * f + P],
                                                   routes["ident"][:])
                    last.then_inc(ht_full, 1)
                if within(k - 1):
                    j, ja, ji = k - 1, 1 - a, (i if a else i - 1)
                    e = expert(j, ja, ji)
                    pe.wait_ge(g_ready, FC * (j + 1))
                    if above(j, 2):
                        pe.wait_ge(y_ready, j - 1)
                    for f in range(FC):
                        nc.tensor.matmul(y_ps[ja][:, 0:C], g_T[ja][:, f, :], experts["w2"][:, f, bass.ds(e, 1), :],
                                         start=f == 0, stop=False)
                    nc.tensor.matmul(y_ps[ja][:, 0:C], routes["ones2"][:], experts["b2"][:, bass.ds(e, 1), :],
                                     start=False, stop=True).then_inc(y_full, 1)
            walk(step, pe, -2, MAX_TILES + 1)

        @block.scalar
        def _(act):
            def step(k, i, a):
                if within(k):
                    e = act.value_load(routes["expert"][0:1, bass.ds(HALF_TILES * a + i, 1)], min_val=0, max_val=E - 1)
                    wait_apart(act, ht_full, k + 1)
                    if above(k, 2):
                        wait_apart(act, y_full, k - 1)
                    for f in range(FC):
                        nc.scalar.activation(g_T[a][:, f, :], ht_ps[a][:, P * f:P * f + P], ACT.Gelu,
                                             bias=experts["ln1_b"][:, f, bass.ds(e, 1)],
                                             scale=experts["ln1_g"][:, f, bass.ds(e, 1)]).then_inc(g_ready, 1)
            walk(step, act, 0, MAX_TILES)

        @block.vector
        def _(dve):
            def step(k, i, a):
                if within(k + 2):
                    j, ja = k + 2, a
                    dve.wait_ge(xt_full, j + 1)
                    if above(j, 2):
                        dve.wait_ge(h_full, j - 1)
                    nc.vector.tensor_copy(x_T[ja][:].rearrange("p k t -> p (k t)"), xt_ps[ja][:, 0:C]
                                          ).then_inc(x_T_ready, 1)
                if within(k + 1):
                    j, ja = k + 1, 1 - a
                    dve.wait_ge(h_full, j + 1)
                    nc.vector.bn_stats(h_stats[ja][:], h_ps[ja][:]).then_inc(stats_done, 1)
                    wait_apart(dve, stats_done, j + 1)
                    nc.vector.bn_aggr(h_mv[ja][:], h_stats[ja][:]).then_inc(mv_done, 1)
                    dve.wait_ge(mv_done, j + 1)
                    nc.vector.tensor_scalar(h_ve[ja][:], h_mv[ja][:, 1:2], EPS, None, ALU.add).then_inc(ve_done, 1)
                if within(k - 1):
                    j, ja, ji = k - 1, 1 - a, (i if a else i - 1)
                    dve.wait_ge(y_full, j + 1)
                    if above(j, 2):
                        dve.wait_ge(y_stored[ja], 16 * ji)
                    nc.vector.tensor_copy(y_out[ja][:], y_ps[ja][:, 0:C]).then_inc(y_ready, 1)
                if within(k + 1):
                    j, ja = k + 1, 1 - a
                    dve.wait_ge(rstd_done, j + 1)
                    if above(j, 2):
                        dve.wait_ge(ht_full, j - 1)
                    nc.vector.tensor_scalar(h_norm[ja][:], h_ps[ja][:], h_mv[ja][:, 0:1], h_rstd[ja][:, 0:1],
                                            ALU.subtract, ALU.mult).then_inc(h_norm_ready, 1)
            nc.vector.memset(routes["minus_half"][:], -0.5).then_inc(begun, 1)
            walk(step, dve, -2, MAX_TILES + 1)


def combine_phase(nc, dram, routes, x1_dram, y_rows, out):
    with ExitStack() as ctx:
        sb = lambda name, shape, dt=F32: ctx.enter_context(nc.sbuf_tensor(name, shape, dt))
        sem = lambda name: ctx.enter_context(nc.semaphore(name))
        y = [[sb(f"y{k}_{a}", [P, CG, C]) for a in range(2)] for k in range(2)]
        x1 = [sb(f"x1_{a}", [P, CG, C]) for a in range(2)]
        f = [sb(f"f_{a}", [P, CG, C]) for a in range(2)]
        g_rep, b_rep = sb("ln_g_rep", [P, C]), sb("ln_b_rep", [P, C])
        stats = sb("c_stats", [P, 2, CG, 6])
        mv = sb("c_mv", [P, 2, CG, 2])
        ve = sb("c_ve", [P, 2, CG])
        rstd = sb("c_rstd", [P, 2, CG])
        half = sb("c_half", [P, CG])
        gb_loaded, mixed = sem("gb_loaded"), sem("mixed")
        x1_loaded = [sem("x1_loaded0"), sem("x1_loaded1")]
        y_loaded = [sem("y_loaded0"), sem("y_loaded1")]
        ve_ready, rstd_ready, out_ready, half_set = sem("c_ve_ready"), sem("c_rstd_ready"), sem("out_ready"), sem("half_set")
        stored = [sem("stored0"), sem("stored1")]
        step = sem("c_step")
        n_groups = TILES // CG
        tiles_of = lambda m: m.rearrange("(n t p) c -> n p t c", t=CG, p=P)
        block = ctx.enter_context(nc.Block())

        @block.sync
        def _(sp):
            sp.dma_start(g_rep[:], dram["ln_g"]).then_inc(gb_loaded, 16)
            sp.dma_start(b_rep[:], dram["ln_b"]).then_inc(gb_loaded, 16)
            for n in range(n_groups):
                a = n % 2
                if n >= 2:
                    sp.wait_ge(out_ready, n - 1)
                sp.dma_start(x1[a][:], tiles_of(x1_dram)[n]).then_inc(x1_loaded[a], 16)
                if n >= 1:
                    sp.wait_ge(out_ready, n)
                    sp.dma_start(tiles_of(out)[n - 1], f[1 - a][:]).then_inc(stored[1 - a], 16)
            sp.wait_ge(out_ready, n_groups)
            sp.dma_start(tiles_of(out)[n_groups - 1], f[1 - n_groups % 2][:]).then_inc(stored[1 - n_groups % 2], 16)
            for a in range(2):
                sp.wait_ge(stored[a], 16 * n_groups // 2)

        @block.gpsimd
        def _(pool):
            nc.gpsimd.memset(half[:], -0.5).then_inc(half_set, 1)
            pool.wait_ge(half_set, 1)

            def fetch(n):
                a = n % 2
                if n >= 2:
                    pool.wait_ge(mixed, n - 1)
                for t in range(CG):
                    for k in range(2):
                        nc.gpsimd.indirect_dma_start(
                            y[k][a][:, t, :], None, y_rows,
                            bass.IndirectOffsetOnAxis(routes["slot"][:, k, CG * n + t:CG * n + t + 1], 0)
                        ).then_inc(y_loaded[a], 16)

            fetch(0)
            for n in range(n_groups):
                if n + 1 < n_groups:
                    fetch(n + 1)
                for i in range(2):
                    pool.wait_ge(ve_ready, 2 * n + i + 1)
                    nc.gpsimd.tensor_tensor(rstd[:, i, :], ve[:, i, :], half[:], ALU.pow).then_inc(rstd_ready, 1)

        @block.vector
        def _(dve):
            steps = [0]

            def mark(ins):
                steps[0] += 1
                ins.then_inc(step, 1)

            def settle():
                dve.wait_ge(step, steps[0])

            def normalise(i, n, src):
                for t in range(CG):
                    mark(nc.vector.bn_stats(stats[:, i, t, :], src[:, t, :]))
                settle()
                for t in range(CG):
                    mark(nc.vector.bn_aggr(mv[:, i, t, :], stats[:, i, t, :]))
                settle()
                nc.vector.tensor_scalar(ve[:, i, :], mv[:, i, :, 1], EPS, None, ALU.add).then_inc(ve_ready, 1)
                dve.wait_ge(rstd_ready, 2 * n + i + 1)

            dve.wait_ge(gb_loaded, 32)
            for n in range(n_groups):
                a = n % 2
                dve.wait_ge(y_loaded[a], 16 * 2 * CG * (n // 2 + 1))
                dve.wait_ge(x1_loaded[a], 16 * (n // 2 + 1))
                if n >= 2:
                    dve.wait_ge(stored[a], 16 * (n // 2))
                for t in range(CG):
                    j = CG * n + t
                    mark(nc.vector.scalar_tensor_tensor(out=f[a][:, t, :], in0=y[0][a][:, t, :],
                                                        scalar=routes["weight"][:, 0, j:j + 1], in1=x1[a][:, t, :],
                                                        op0=ALU.mult, op1=ALU.add))
                settle()
                for t in range(CG):
                    j = CG * n + t
                    last = nc.vector.scalar_tensor_tensor(out=f[a][:, t, :], in0=y[1][a][:, t, :],
                                                          scalar=routes["weight"][:, 1, j:j + 1], in1=f[a][:, t, :],
                                                          op0=ALU.mult, op1=ALU.add)
                    if t < CG - 1:
                        mark(last)
                last.then_inc(mixed, 1)
                dve.wait_ge(mixed, n + 1)
                normalise(0, n, f[a])
                for t in range(CG):
                    mark(nc.vector.tensor_scalar(f[a][:, t, :], f[a][:, t, :], mv[:, 0, t, 0:1], rstd[:, 0, t:t + 1],
                                                 ALU.subtract, ALU.mult))
                settle()
                rep = [P, CG, C]
                mark(nc.vector.tensor_tensor(f[a][:], f[a][:], g_rep[:].unsqueeze(1).to_broadcast(rep), ALU.mult))
                mark(nc.vector.tensor_tensor(x1[a][:], x1[a][:], b_rep[:].unsqueeze(1).to_broadcast(rep), ALU.add))
                settle()
                mark(nc.vector.tensor_tensor(f[a][:], f[a][:], x1[a][:], ALU.add))
                settle()
                normalise(1, n, f[a])
                for t in range(CG):
                    last = nc.vector.tensor_scalar(f[a][:, t, :], f[a][:, t, :], mv[:, 1, t, 0:1],
                                                   rstd[:, 1, t:t + 1], ALU.subtract, ALU.mult)
                    if t < CG - 1:
                        mark(last)
                last.then_inc(out_ready, 1)


def attention_weights(ctx, nc, routes):
    sb = lambda name, shape, dt=F32: ctx.enter_context(nc.sbuf_tensor(name, shape, dt))
    wts = {"lat_hi": sb("lat_hi", [P, KC, 2, NH * L], F32R), "lat_lo": sb("lat_lo", [P, KC, 2, NH * L], F32R),
           "lat_bias": sb("lat_bias", [P, 2, GROUPS]), "vo_hi": sb("vo_hi", [P, KC, C], F32R),
           "vo_lo": sb("vo_lo", [P, KC, C], F32R), "vo_bias": sb("vo_bias", [P, C]), "wqk": sb("wqk", [P, P]),
           "q_bias": sb("q_bias", [P, 1]), "cproj": sb("cproj_w", [P, GROUPS, C]), "eps": sb("eps", [P, 1]),
           "gate": sb("gate_w", [P, KC, E])}
    consts = {"cos": sb("cos", [P, T]), "sin": sb("sin", [P, T]), "ident": routes["ident"],
              "ident_bf": sb("ident_bf", [P, P], BF16), "mask": sb("mask", [P, P], BF16),
              "mask_T": sb("mask_T", [P, P], BF16)}
    return wts, consts


def build(nc, dram, out):
    dram = {k: ap.bitcast(BF16) if k in BF16_BITS else ap for k, ap in dram.items()}
    x1 = nc.dram_tensor("x1", (B, T, C), F32).ap()
    logits = nc.dram_tensor("gate_logits", (B, TB, P, E), F32).ap()
    token_of_slot = nc.dram_tensor("token_of_slot", (MAX_TILES * P, 1), I32).ap()
    y_rows = nc.dram_tensor("y_rows", (MAX_TILES * P, C), F32).ap()
    with ExitStack() as ctx:
        sb = lambda name, shape, dt=F32: ctx.enter_context(nc.sbuf_tensor(name, shape, dt))
        routes = {"ident": sb("ident", [P, P])}
        with ExitStack() as attention:
            wts, consts = attention_weights(attention, nc, routes)
            weight_phase(nc, dram, wts, consts)
            attention_phase(nc, dram, wts, consts, x1, logits)
        routes.update({"weight": sb("weight", [P, 2, TILES]), "slot": sb("slot", [P, 2, TILES], I32)})
        with ExitStack() as ffn:
            sb = lambda name, shape, dt=F32: ffn.enter_context(nc.sbuf_tensor(name, shape, dt))
            routes.update({"expert": sb("expert", [1, MAX_TILES], I32), "token": sb("token", [P, 2, HALF_TILES], I32),
                           "split": sb("split", [2, 2]), "ones2": sb("ones2", [2, P], F32R),
                           "minus_half": sb("minus_half", [P, 1])})
            experts = {"w1": sb("w1", [P, KC, E, H]), "w2": sb("w2", [P, FC, E, C]), "b1": sb("b1", [2, E, H], F32R),
                       "b2": sb("b2", [2, E, C], F32R), "ln1_g": sb("ln1_g", [P, FC, E]),
                       "ln1_b": sb("ln1_b", [P, FC, E])}
            routing_phase(nc, dram, logits, experts, routes, token_of_slot)
            expert_phase(nc, experts, routes, x1.rearrange("b t c -> (b t) c"), y_rows)
        combine_phase(nc, dram, routes, x1.rearrange("b t c -> (b t) c"), y_rows, out.rearrange("b t c -> (b t) c"))


def ffn_layouts(a):
    w1, w2 = a["L0_ffn_w1"], a["L0_ffn_w2"]
    b12 = np.concatenate([a["L0_ffn_b1"], a["L0_ffn_b2"]], 1)
    p = np.arange(P)
    cols = lambda m: m.reshape(E, FC, P).transpose(2, 1, 0)
    return {
        "gate": a["L0_ffn_gate_w"].reshape(KC, P, E).transpose(1, 0, 2),
        "w1": w1.reshape(E, KC, P, H).transpose(2, 1, 0, 3), "w2": w2.reshape(E, FC, P, C).transpose(2, 1, 0, 3),
        "b12": np.repeat(b12[None], 2, 0), "ln1_g": cols(a["L0_ffn_ln1_g"]), "ln1_b": cols(a["L0_ffn_ln1_b"]),
        "ln_g": np.repeat(a["L0_ffn_ln_g"][None], P, 0), "ln_b": np.repeat(a["L0_ffn_ln_b"][None], P, 0),
        "split": np.eye(2, dtype=np.float32),
        "rank": np.repeat(np.arange(E, 0, -1, dtype=np.float32)[None], P, 0),
        "limit": np.repeat(P * np.arange(TILES, dtype=np.float32)[None], P, 0),
        "slot_no": np.repeat(np.arange(MAX_TILES, dtype=np.float32)[None], P, 0),
        "ids": (P * np.arange(TILES)[None] + p[:, None]).astype(np.int32),
        "before": bf16_bits(p[:, None] < p[None]),
        "ones": bf16_bits(np.ones((P, P))),
    }


def rope_tables():
    inv = (np.float32(1.0) / np.float32(10000.0) ** (np.arange(0, L, 2, dtype=np.float32) / np.float32(L)))
    freq = np.outer(np.arange(T, dtype=np.float32), inv.astype(np.float32)).astype(np.float32)
    cos = np.repeat(np.cos(freq), 2, axis=1).T
    sin = np.repeat(np.sin(freq), 2, axis=1).T * np.tile(np.array([-1, 1], np.float32), L // 2)[:, None]
    return np.tile(cos, (HG, 1)).astype(np.float32), np.tile(sin, (HG, 1)).astype(np.float32)


def block_diag(a, n):
    out = np.zeros((n * a.shape[0], n * a.shape[1]), a.dtype)
    for i in range(n):
        out[i * a.shape[0]:(i + 1) * a.shape[0], i * a.shape[1]:(i + 1) * a.shape[1]] = a
    return out


def bf16_bits(a):
    return (np.ascontiguousarray(a, dtype=np.float32).view(np.uint32) >> 16).astype(np.uint16)


def layouts(i):
    a = {k: np.asarray(v) for k, v in i.items()}
    rows = lambda m: np.ascontiguousarray(m.reshape(-1, P, m.shape[-1]).transpose(1, 0, 2))
    q2l, kv2l, l2o = a["L0_attn_q2l_w"], a["L0_attn_kv2l_w"], a["L0_attn_l2o_w"]
    cproj_T = a["L0_attn_cproj_w"].T.reshape(GROUPS, HG, HD, C)
    cproj = np.zeros((GROUPS, HG, 2 * HD, C), np.float32)
    cproj[:, :, :HD] = cproj_T
    cproj[0, 0, HD] = a["L0_attn_cproj_b"]
    bq = a["L0_attn_c_attn_b"].reshape(6, P)
    cos, sin = rope_tables()
    keep = np.arange(P)[:, None] >= np.arange(P)[None, :]
    mask = bf16_bits(np.where(keep, 0.0, NEG))
    d = {
        "x": a["L0_attn_x"], "xT": np.ascontiguousarray(a["L0_attn_x"].transpose(0, 2, 1)),
        "w_nat": rows(a["L0_attn_c_attn_w"]),
        "bd_lat": np.ascontiguousarray(np.stack([block_diag(q2l.T, 8), block_diag(kv2l.T, 8)], 1)),
        "kv_bd": rows(block_diag(kv2l, 8)), "lo_bd": rows(block_diag(l2o.T, 8)),
        "b_cols": np.ascontiguousarray(bq.T),
        "lat_b": np.stack([np.tile(a["L0_attn_q2l_b"], HG), np.tile(a["L0_attn_kv2l_b"], HG)], 1),
        "bv_rep": np.ascontiguousarray(np.repeat(bq[4:6].T[:, :, None], P, 2)),
        "kvb_rep": rows(np.repeat(np.tile(a["L0_attn_kv2l_b"], 8)[:, None], P, 1)),
        "lo_b": np.repeat(np.tile(a["L0_attn_l2o_b"], NH)[None], P, 0),
        "wqk_bd": block_diag(a["L0_attn_wqk_w"].T, HG), "wqk_b": np.tile(a["L0_attn_wqk_b"], HG)[:, None],
        "cproj": np.ascontiguousarray(cproj.reshape(GROUPS, P, C).transpose(1, 0, 2)),
        "cos": cos, "sin": sin, "ident": np.eye(P, dtype=np.float32),
        "ident_bf": bf16_bits(np.eye(P)),
        "mask": mask, "mask_T": np.ascontiguousarray(mask.T),
    }
    d.update(ffn_layouts(a))
    return {k: np.ascontiguousarray(v) for k, v in d.items()}


def kernel(**inputs):
    import concourse.bacc as bacc
    from concourse.bass_utils import run_bass_kernel_spmd

    nc = bacc.Bacc("TRN2", target_bir_lowering=False, num_devices=1)
    arrays = layouts(inputs)
    dram = {k: nc.dram_tensor("in_" + k, v.shape, mybir.dt.from_np(v.dtype), kind="ExternalInput").ap()
            for k, v in arrays.items()}
    out = nc.dram_tensor("out", (B, T, C), F32, kind="ExternalOutput").ap()
    build(nc, dram, out)
    r = run_bass_kernel_spmd(nc, [{"in_" + k: v for k, v in arrays.items()}], core_ids=[0])
    return r.results[0]["out"]
```
